# Optimizing a Trainium2 kernel written in Bass

```python
import numpy as np
import jax
import jax.numpy as jnp

def _softmax(x, axis=-1):
    return jax.nn.softmax(x, axis=axis)

def _gelu(x):
    return jax.nn.gelu(x, approximate=True)

def _silu(x):
    return jax.nn.silu(x)

def _sigmoid(x):
    return jax.nn.sigmoid(x)

def _layernorm(x, axis=-1, eps=1e-05):
    m = jnp.mean(x, axis=axis, keepdims=True)
    v = jnp.var(x, axis=axis, keepdims=True)
    return (x - m) / jnp.sqrt(v + eps)

def _scatter_add(tgt, idx, src, axis=0):
    return tgt.at[idx].add(src)

def _segment_sum(src, seg, n):
    return jax.ops.segment_sum(src, seg, n)
kernel_name = 'mk_dlrm_tower_d1_rec_r8_dc2d2c'

def setup_inputs(seed: int=0):
    np.random.seed(seed)
    _w = jnp.asarray

    def _rec_inputs():
        import jax
        import jax.numpy as jnp
        _tk = jax.random.key(seed)
        ids = jnp.stack([jax.random.randint(jax.random.fold_in(_tk, 200 + f), (512,), 0, v, jnp.int32) for f, v in enumerate([1250, 125000, 1250, 1250, 1000, 1250, 1250, 1000, 1000, 1250, 1250, 1000, 1000, 12500, 1250, 1000, 1250, 1250, 1250, 12500, 1000, 1000, 1000, 12500, 1250, 1000])], axis=1)
        tbl_0 = 0.05 * jax.random.normal(jax.random.fold_in(_tk, 500 + 0), (1250, 128), jnp.float32)
        tbl_1 = 0.05 * jax.random.normal(jax.random.fold_in(_tk, 500 + 1), (125000, 128), jnp.float32)
        tbl_2 = 0.05 * jax.random.normal(jax.random.fold_in(_tk, 500 + 2), (1250, 128), jnp.float32)
        tbl_3 = 0.05 * jax.random.normal(jax.random.fold_in(_tk, 500 + 3), (1250, 128), jnp.float32)
        tbl_4 = 0.05 * jax.random.normal(jax.random.fold_in(_tk, 500 + 4), (1000, 128), jnp.float32)
        tbl_5 = 0.05 * jax.random.normal(jax.random.fold_in(_tk, 500 + 5), (1250, 128), jnp.float32)
        tbl_6 = 0.05 * jax.random.normal(jax.random.fold_in(_tk, 500 + 6), (1250, 128), jnp.float32)
        tbl_7 = 0.05 * jax.random.normal(jax.random.fold_in(_tk, 500 + 7), (1000, 128), jnp.float32)
        tbl_8 = 0.05 * jax.random.normal(jax.random.fold_in(_tk, 500 + 8), (1000, 128), jnp.float32)
        tbl_9 = 0.05 * jax.random.normal(jax.random.fold_in(_tk, 500 + 9), (1250, 128), jnp.float32)
        tbl_10 = 0.05 * jax.random.normal(jax.random.fold_in(_tk, 500 + 10), (1250, 128), jnp.float32)
        tbl_11 = 0.05 * jax.random.normal(jax.random.fold_in(_tk, 500 + 11), (1000, 128), jnp.float32)
        tbl_12 = 0.05 * jax.random.normal(jax.random.fold_in(_tk, 500 + 12), (1000, 128), jnp.float32)
        tbl_13 = 0.05 * jax.random.normal(jax.random.fold_in(_tk, 500 + 13), (12500, 128), jnp.float32)
        tbl_14 = 0.05 * jax.random.normal(jax.random.fold_in(_tk, 500 + 14), (1250, 128), jnp.float32)
        tbl_15 = 0.05 * jax.random.normal(jax.random.fold_in(_tk, 500 + 15), (1000, 128), jnp.float32)
        tbl_16 = 0.05 * jax.random.normal(jax.random.fold_in(_tk, 500 + 16), (1250, 128), jnp.float32)
        tbl_17 = 0.05 * jax.random.normal(jax.random.fold_in(_tk, 500 + 17), (1250, 128), jnp.float32)
        tbl_18 = 0.05 * jax.random.normal(jax.random.fold_in(_tk, 500 + 18), (1250, 128), jnp.float32)
        tbl_19 = 0.05 * jax.random.normal(jax.random.fold_in(_tk, 500 + 19), (12500, 128), jnp.float32)
        tbl_20 = 0.05 * jax.random.normal(jax.random.fold_in(_tk, 500 + 20), (1000, 128), jnp.float32)
        tbl_21 = 0.05 * jax.random.normal(jax.random.fold_in(_tk, 500 + 21), (1000, 128), jnp.float32)
        tbl_22 = 0.05 * jax.random.normal(jax.random.fold_in(_tk, 500 + 22), (1000, 128), jnp.float32)
        tbl_23 = 0.05 * jax.random.normal(jax.random.fold_in(_tk, 500 + 23), (12500, 128), jnp.float32)
        tbl_24 = 0.05 * jax.random.normal(jax.random.fold_in(_tk, 500 + 24), (1250, 128), jnp.float32)
        tbl_25 = 0.05 * jax.random.normal(jax.random.fold_in(_tk, 500 + 25), (1000, 128), jnp.float32)
        _rk = jax.random.fold_in(_tk, 7)
        r_dense = -0.000520686 + 1.00062 * jax.random.normal(jax.random.fold_in(_rk, 101), (512, 128), jnp.float32)
        W_top1 = 0.0456912 * jax.random.normal(jax.random.fold_in(_tk, 801), (479, 512), jnp.float32)
        W_top2 = 0.0441942 * jax.random.normal(jax.random.fold_in(_tk, 802), (512, 256), jnp.float32)
        W_top3 = 0.0625 * jax.random.normal(jax.random.fold_in(_tk, 803), (256, 1), jnp.float32)
        b_top1 = jnp.zeros((512,), jnp.float32)
        b_top2 = jnp.zeros((256,), jnp.float32)
        return (r_dense, ids, tbl_0, tbl_1, tbl_2, tbl_3, tbl_4, tbl_5, tbl_6, tbl_7, tbl_8, tbl_9, tbl_10, tbl_11, tbl_12, tbl_13, tbl_14, tbl_15, tbl_16, tbl_17, tbl_18, tbl_19, tbl_20, tbl_21, tbl_22, tbl_23, tbl_24, tbl_25, W_top1, b_top1, W_top2, b_top2, W_top3)
    r_dense, ids, tbl_0, tbl_1, tbl_2, tbl_3, tbl_4, tbl_5, tbl_6, tbl_7, tbl_8, tbl_9, tbl_10, tbl_11, tbl_12, tbl_13, tbl_14, tbl_15, tbl_16, tbl_17, tbl_18, tbl_19, tbl_20, tbl_21, tbl_22, tbl_23, tbl_24, tbl_25, W_top1, b_top1, W_top2, b_top2, W_top3 = _rec_inputs()

    def _L0_rec_setup():
        import jax, jax.numpy as jnp
        import numpy as np
        B, NUM_EMBS, D = (2048, 26, 128)
        key = jax.random.key(seed)
        k1, k2 = jax.random.split(key)
        dense = jax.random.normal(k1, (B, D), dtype=jnp.float32)
        embs = jax.random.normal(k2, (B, NUM_EMBS, D), dtype=jnp.float32)
        return {'dense': dense, 'embs': embs}
    _L0_rec_all = _L0_rec_setup()
    _L0_rec_in = {k: v for k, v in _L0_rec_all.items() if k in ()}
    del _L0_rec_all
    return {'r_dense': r_dense, 'ids': ids, 'tbl_0': tbl_0, 'tbl_1': tbl_1, 'tbl_2': tbl_2, 'tbl_3': tbl_3, 'tbl_4': tbl_4, 'tbl_5': tbl_5, 'tbl_6': tbl_6, 'tbl_7': tbl_7, 'tbl_8': tbl_8, 'tbl_9': tbl_9, 'tbl_10': tbl_10, 'tbl_11': tbl_11, 'tbl_12': tbl_12, 'tbl_13': tbl_13, 'tbl_14': tbl_14, 'tbl_15': tbl_15, 'tbl_16': tbl_16, 'tbl_17': tbl_17, 'tbl_18': tbl_18, 'tbl_19': tbl_19, 'tbl_20': tbl_20, 'tbl_21': tbl_21, 'tbl_22': tbl_22, 'tbl_23': tbl_23, 'tbl_24': tbl_24, 'tbl_25': tbl_25, 'W_top1': W_top1, 'b_top1': b_top1, 'W_top2': W_top2, 'b_top2': b_top2, 'W_top3': W_top3}

def reference(r_dense, ids, tbl_0, tbl_1, tbl_2, tbl_3, tbl_4, tbl_5, tbl_6, tbl_7, tbl_8, tbl_9, tbl_10, tbl_11, tbl_12, tbl_13, tbl_14, tbl_15, tbl_16, tbl_17, tbl_18, tbl_19, tbl_20, tbl_21, tbl_22, tbl_23, tbl_24, tbl_25, W_top1, b_top1, W_top2, b_top2, W_top3):
    import jax
    import jax.numpy as jnp

    def _L0_rec_ref(dense, embs):
        import jax, jax.numpy as jnp
        import numpy as np
        B, NUM_EMBS, D = (2048, 26, 128)
        T = jnp.concatenate([dense[:, None, :], embs], axis=1)
        N = T.shape[1]
        Z = jnp.einsum('bnd,bmd->bnm', T, T)
        iu0, iu1 = jnp.triu_indices(N, k=1)
        return Z[:, iu0, iu1]
    e = jnp.stack([tbl_0[ids[:, 0]], tbl_1[ids[:, 1]], tbl_2[ids[:, 2]], tbl_3[ids[:, 3]], tbl_4[ids[:, 4]], tbl_5[ids[:, 5]], tbl_6[ids[:, 6]], tbl_7[ids[:, 7]], tbl_8[ids[:, 8]], tbl_9[ids[:, 9]], tbl_10[ids[:, 10]], tbl_11[ids[:, 11]], tbl_12[ids[:, 12]], tbl_13[ids[:, 13]], tbl_14[ids[:, 14]], tbl_15[ids[:, 15]], tbl_16[ids[:, 16]], tbl_17[ids[:, 17]], tbl_18[ids[:, 18]], tbl_19[ids[:, 19]], tbl_20[ids[:, 20]], tbl_21[ids[:, 21]], tbl_22[ids[:, 22]], tbl_23[ids[:, 23]], tbl_24[ids[:, 24]], tbl_25[ids[:, 25]]], axis=1)
    z = _L0_rec_ref(r_dense, e)
    z = z.reshape(z.shape[0], -1)
    h = jnp.concatenate([z, r_dense], axis=1)
    h = jnp.maximum(h @ W_top1 + b_top1, 0.0)
    h = jnp.maximum(h @ W_top2 + b_top2, 0.0)
    y = h @ W_top3
    return y

_drawn_inputs = setup_inputs


def setup_inputs(seed=0):
    import zlib

    import numpy as np

    out = dict(_drawn_inputs(seed))
    spreads = {'b_top1': (0.0, 0.1), 'b_top2': (0.0, 0.1)}
    factors = {}
    for name, (base, spread) in spreads.items():
        noise = np.random.default_rng([zlib.crc32(name.encode()), seed]).standard_normal(out[name].shape)
        drawn = base * np.exp(spread * noise) if base else spread * noise
        out[name] = jnp.asarray(drawn.astype(out[name].dtype))
    for name, factor in factors.items():
        out[name] = (out[name] * factor).astype(out[name].dtype)
    return out
```

```python
from contextlib import ExitStack

import concourse.bass as bass
from concourse import mybir

VOCABS = [1250, 125000, 1250, 1250, 1000, 1250, 1250, 1000, 1000, 1250, 1250, 1000, 1000, 12500, 1250, 1000,
          1250, 1250, 1250, 12500, 1000, 1000, 1000, 12500, 1250, 1000]
P = 128
B = 512
F = len(VOCABS)
V = F + 1
HALF = 64
TILE = 2 * HALF
TILES = B // TILE
CHUNKS = HALF * F // P
PIECES = 4
PS = HALF // PIECES
OWN = PS * F // P
GROUP = 4
GROUPS = PS // GROUP
QUAD = 32
SLOTS = (F + 3) // 4
H1, H2 = 512, 256
N1, N2 = H1 // P, H2 // P
BANK = 512


def program(nc, table, ids, row_base, dense_t, w1_pairs, w1_dense, b1, w2, b2, w3, y):
    f32, i32, u32 = mybir.dt.float32, mybir.dt.int32, mybir.dt.uint32
    ALU = mybir.AluOpType
    ACT = mybir.ActivationFunctionType

    with ExitStack() as ctx:
        def sb(name, shape, dt=f32):
            return ctx.enter_context(nc.sbuf_tensor(name, shape, dt))

        def ps(name, shape):
            return ctx.enter_context(nc.psum_tensor(name, shape, f32))

        def sem(name):
            return ctx.enter_context(nc.semaphore(name))

        ids_sb = sb("ids_sb", [P, B // HALF, CHUNKS], i32)
        base_sb = sb("base_sb", [P, CHUNKS], i32)
        all_rows = sb("all_rows", [P, B // HALF, CHUNKS], i32)
        rows = sb("rows", [P, 2, CHUNKS], i32)
        gathered = sb("gathered", [P, 2, CHUNKS, P])
        ident = sb("ident", [P, P])
        dense_sb = sb("dense_sb", [P, B])
        vecs = sb("vecs", [P, 2, HALF, QUAD])
        pairs = sb("pairs", [P, SLOTS, TILE])
        w1p_sb = sb("w1p_sb", [P, SLOTS, H1])
        w1d_sb = sb("w1d_sb", [P, H1])
        b1_sb = sb("b1_sb", [P, N1])
        w2_sb = sb("w2_sb", [P, N1, H2])
        b2_sb = sb("b2_sb", [P, N2])
        w3_sb = sb("w3_sb", [P, N2])
        h1_sb = sb("h1_sb", [P, N1, TILE])
        h2_sb = sb("h2_sb", [P, N2, TILE])
        y_sb = sb("y_sb", [1, B])

        turned = ps("turned", [P, PIECES, BANK])
        dots = ps("dots", [P, 2, GROUPS, P])
        h1_ps = ps("h1_ps", [P, 2, BANK])
        h2_ps = turned[:, 0:N2, 0:TILE]
        y_ps = turned[0:1, N2, 0:TILE]

        ids_in = sem("ids_in")
        base_in = sem("base_in")
        dense_in = sem("dense_in")
        w1_in = sem("w1_in")
        w2_in = sem("w2_in")
        ident_zero = sem("ident_zero")
        ident_ready = sem("ident_ready")
        rows_found = sem("rows_found")
        half_begun = sem("half_begun")
        rows_ready = sem("rows_ready")
        landed = [sem(f"landed{c}") for c in range(2 * CHUNKS)]
        turned_ready = sem("turned_ready")
        vecs_dve = sem("vecs_dve")
        vecs_act = sem("vecs_act")
        dense_cols = sem("dense_cols")
        dots_ready = sem("dots_ready")
        vecs_zero = sem("vecs_zero")
        pairs_dve = sem("pairs_dve")
        pairs_act = sem("pairs_act")
        h1_low = sem("h1_low")
        pairs_free = sem("pairs_free")
        h1_dve = sem("h1_dve")
        h1_act = sem("h1_act")
        h2_sum = sem("h2_sum")
        h2_dve = sem("h2_dve")
        h2_act = sem("h2_act")
        y_sum = sem("y_sum")
        y_ready = sem("y_ready")
        stored = sem("stored")

        def piece_parts(k):
            for i in range(OWN):
                yield 1 + OWN * k + i, 0, P, i * P
            yield 0, QUAD * k, QUAD * (k + 1), OWN * P

        def evacuate(copy, half, k):
            src = turned[:, k, 0:PS * F].rearrange("p (s f) -> p s f", f=F)
            return copy(vecs[:, half, k * PS:(k + 1) * PS, 0:F], src)

        def spread(copy, half, k, quads):
            for j in quads:
                for q in range(4):
                    n = (F - q + 3) // 4
                    s0 = half * HALF + k * PS + j
                    cols = dots[QUAD * j:QUAD * j + F, k % 2, :, V * j + 1 + q:V * j + 1 + q + 4 * (n - 1) + 1:4]
                    dst = pairs[QUAD * q:QUAD * q + F, 0:n, s0:s0 + PS - GROUP + 1:GROUP]
                    last = copy(dst, cols.rearrange("p g t -> p t g"))
            return last

        block = ctx.enter_context(nc.Block())

        @block.sync
        def _(sp):
            sp.dma_start(ids_sb[:, :], ids).then_inc(ids_in, 16)
            sp.dma_start(dense_sb[:, :], dense_t).then_inc(dense_in, 16)
            sp.dma_start(w1p_sb[:, :, :], w1_pairs).then_inc(w1_in, 16)
            sp.dma_start(w1d_sb[:, :], w1_dense).then_inc(w1_in, 16)
            sp.dma_start(w2_sb[:, :, :], w2).then_inc(w2_in, 16)
            sp.wait_ge(y_ready, TILES + 1)
            sp.dma_start(y, y_sb[:, :]).then_inc(stored, 16)
            sp.wait_ge(stored, 16)

        @block.gpsimd
        def _(pool):
            nc.gpsimd.memset(ident[:, :], 0.0).then_inc(ident_zero, 1)
            pool.wait_ge(ident_zero, 1)
            nc.gpsimd.affine_select(out=ident[:, :], in_=ident[:, :], compare_op=ALU.not_equal, fill=1.0,
                                    base=0, pattern=[[-1, P]], channel_multiplier=1).then_inc(ident_ready, 1)
            with pool.Fori(0, TILES) as t:
                for half in range(2):
                    pool.wait_ge(rows_ready, 2 * t + half + 1)
                    pool.sem_inc(half_begun, 1)
                    for c in range(CHUNKS):
                        nc.gpsimd.indirect_dma_start(
                            gathered[:, half, c, :], None, table,
                            bass.IndirectOffsetOnAxis(rows[:, half, c:c + 1].bitcast(u32), 0),
                        ).then_inc(landed[half * CHUNKS + c], 16)

        @block.tensor
        def _(pe):
            def transposes(t, half, k):
                if k == 0:
                    pe.wait_ge(landed[half * CHUNKS], 16 * t + 16)
                for c, a, b, col in piece_parts(k):
                    if c:
                        pe.wait_ge(landed[half * CHUNKS + c], 16 * t + 16)
                    last = nc.tensor.transpose(turned[:, k, col:col + b - a], gathered[a:b, half, c, :],
                                               ident[a:b, a:b])
                last.then_inc(turned_ready, 1)

            def dot_products(t, half, k):
                n = 8 * t + 4 * half + k
                pe.wait_ge((vecs_dve, vecs_act)[k % 2], 4 * t + 2 * half + k // 2 + 1)
                if 4 * half + k >= 2:
                    pe.wait_ge(pairs_dve, n - 1)
                    pe.wait_ge(pairs_act, n - 1)
                for g in range(GROUPS):
                    at = k * PS + g * GROUP
                    group = vecs[:, half, at:at + GROUP, :]
                    last = nc.tensor.matmul(dots[:, k % 2, g, 0:GROUP * V], group.rearrange("p s v -> p (s v)"),
                                            group[:, :, 0:V], start=True, stop=True)
                last.then_inc(dots_ready, 1)

            def mlp(t, passes, half, halves):
                lo, n = half * HALF, halves * HALF
                pieces = 8 * t + 4 * (half + halves)
                pe.wait_ge(pairs_dve, pieces)
                pe.wait_ge(pairs_act, pieces)
                dense = vecs[:, half:half + halves, :, F]
                for i in range(N1):
                    units = h1_ps[:, i // 2, i % 2 * TILE:i % 2 * TILE + n]
                    nc.tensor.matmul(units, w1d_sb[:, i * P:(i + 1) * P], dense, start=True, stop=False)
                    for s in range(SLOTS):
                        last = nc.tensor.matmul(units, w1p_sb[:, s, i * P:(i + 1) * P],
                                                pairs[:, s, lo:lo + n], start=False, stop=s == SLOTS - 1)
                    if i % 2:
                        last.then_inc((h1_low, pairs_free)[i // 2], 1)
                pe.wait_ge(h1_dve, passes + 1)
                pe.wait_ge(h1_act, passes + 1)
                for o in range(N2):
                    for i in range(N1):
                        last = nc.tensor.matmul(h2_ps[:, o, 0:n], w2_sb[:, i, o * P:(o + 1) * P],
                                                h1_sb[:, i, 0:n], start=i == 0, stop=i == N1 - 1)
                    last.then_inc(h2_sum, 1)
                pe.wait_ge(h2_dve, passes + 1)
                pe.wait_ge(h2_act, passes + 1)
                for o in range(N2):
                    last = nc.tensor.matmul(y_ps[0:1, 0:n], w3_sb[:, o:o + 1], h2_sb[:, o, 0:n],
                                            start=o == 0, stop=o == N2 - 1)
                last.then_inc(y_sum, 1)
                pe.wait_ge(y_ready, passes + 1)

            def half_tile(t, half):
                transposes(t, half, 0)
                for k in range(1, PIECES):
                    transposes(t, half, k)
                    if k == 1 and half == 0:
                        pe.wait_ge(dense_cols, t + 1)
                    dot_products(t, half, k - 1)
                dot_products(t, half, PIECES - 1)

            pe.wait_ge(ident_ready, 1)
            pe.wait_ge(vecs_zero, 1)
            pe.wait_ge(w1_in, 32)
            pe.wait_ge(w2_in, 64)
            with pe.Fori(0, TILES - 1) as t:
                half_tile(t, 0)
                half_tile(t, 1)
                mlp(t, t, 0, 2)
            half_tile(TILES - 1, 0)
            mlp(TILES - 1, TILES - 1, 0, 1)
            half_tile(TILES - 1, 1)
            mlp(TILES - 1, TILES, 1, 1)

        @block.vector
        def _(dve):
            copy = nc.vector.tensor_copy

            def place_rows(t, half):
                copy(rows[:, half, :], all_rows[:, bass.ds(2 * t + half, 1), :].rearrange("p a c -> p (a c)")
                     ).then_inc(rows_ready, 1)

            def half_tile(t, half):
                def vectors(k):
                    dve.wait_ge(turned_ready, 8 * t + 4 * half + k + 1)
                    evacuate(copy, half, k).then_inc(vecs_dve, 1)

                def products(k):
                    dve.wait_ge(dots_ready, 8 * t + 4 * half + k + 1)
                    spread(copy, half, k, (0, 1)).then_inc(pairs_dve, 1)

                vectors(0)
                if half == 0:
                    dve.wait_ge(pairs_free, t + 1)
                products(0)
                vectors(2)
                products(1)
                products(2)
                products(PIECES - 1)

            def mlp(passes, n, y_at):
                dve.wait_ge(h1_low, passes + 1)
                for i in (0, 1):
                    last = nc.vector.tensor_scalar(h1_sb[:, i, 0:n], h1_ps[:, 0, i * TILE:i * TILE + n],
                                                   b1_sb[:, i:i + 1], 0.0, ALU.add, ALU.max)
                last.then_inc(h1_dve, 1)
                dve.wait_ge(h2_sum, N2 * passes + 1)
                nc.vector.tensor_scalar(h2_sb[:, 0, 0:n], h2_ps[:, 0, 0:n], b2_sb[:, 0:1], 0.0,
                                        ALU.add, ALU.max).then_inc(h2_dve, 1)
                dve.wait_ge(y_sum, passes + 1)
                copy(y_sb[0:1, bass.ds(y_at, n)], y_ps[0:1, 0:n]).then_inc(y_ready, 1)

            dve.wait_ge(ids_in, 16)
            dve.wait_ge(base_in, 16)
            base_all = base_sb[:, :].unsqueeze(1).to_broadcast([P, B // HALF, CHUNKS])
            nc.vector.tensor_tensor(all_rows[:, :, :], ids_sb[:, :, :], base_all, ALU.add).then_inc(rows_found, 1)
            dve.wait_ge(rows_found, 1)
            place_rows(0, 0)
            place_rows(0, 1)
            nc.vector.memset(pairs[:, :, :], 0.0).then_inc(pairs_free, 1)
            nc.vector.memset(vecs[:, :, :, :], 0.0).then_inc(vecs_zero, 1)
            dve.wait_ge(vecs_zero, 1)
            dve.wait_ge(w2_in, 64)
            with dve.Fori(0, TILES - 1) as t:
                for half in range(2):
                    half_tile(t, half)
                    place_rows(t + 1, half)
                mlp(t, TILE, t * TILE)
            t = TILES - 1
            for half in range(2):
                half_tile(t, half)
                mlp(t + half, HALF, t * TILE + half * HALF)

        @block.scalar
        def _(act):
            def copy(dst, src):
                return nc.scalar.activation(dst, src, ACT.Copy)

            act.dma_start(base_sb[:, :], row_base).then_inc(base_in, 16)
            act.dma_start(b1_sb[:, :], b1).then_inc(w2_in, 16)
            act.dma_start(b2_sb[:, :], b2).then_inc(w2_in, 16)
            act.dma_start(w3_sb[:, :], w3).then_inc(w2_in, 16)

            def half_tile(t, half):
                def vectors(k):
                    act.wait_ge(turned_ready, 8 * t + 4 * half + k + 1)
                    evacuate(copy, half, k).then_inc(vecs_act, 1)

                def products(k):
                    act.wait_ge(dots_ready, 8 * t + 4 * half + k + 1)
                    spread(copy, half, k, (2, 3)).then_inc(pairs_act, 1)

                if half == 0:
                    act.wait_ge(pairs_free, t + 1)
                    src = dense_sb[:, bass.ds(t * TILE, TILE)].rearrange("p (h s) -> p h s", h=2)
                    copy(vecs[:, :, :, F], src).then_inc(dense_cols, 1)
                vectors(1)
                products(0)
                products(1)
                vectors(3)
                products(2)
                products(PIECES - 1)

            def mlp(passes, n):
                act.wait_ge(pairs_free, passes + 2)
                for i in (2, 3):
                    last = nc.scalar.activation(h1_sb[:, i, 0:n], h1_ps[:, 1, (i - 2) * TILE:(i - 2) * TILE + n],
                                                ACT.Relu, bias=b1_sb[:, i:i + 1])
                last.then_inc(h1_act, 1)
                act.wait_ge(h2_sum, N2 * passes + 2)
                nc.scalar.activation(h2_sb[:, 1, 0:n], h2_ps[:, 1, 0:n], ACT.Relu,
                                     bias=b2_sb[:, 1:2]).then_inc(h2_act, 1)

            act.wait_ge(dense_in, 16)
            act.wait_ge(vecs_zero, 1)
            act.wait_ge(w2_in, 64)
            with act.Fori(0, TILES - 1) as t:
                half_tile(t, 0)
                half_tile(t, 1)
                mlp(t, TILE)
            half_tile(TILES - 1, 0)
            mlp(TILES - 1, HALF)
            half_tile(TILES - 1, 1)
            mlp(TILES, HALF)


def kernel(**inputs):
    import numpy as np
    import concourse.bacc as bacc
    from concourse.bass_utils import run_bass_kernel_spmd

    x = {name: np.asarray(a) for name, a in inputs.items()}

    def chunked(a):
        a = a.reshape(-1, PIECES, PS * F)
        own = a[:, :, :OWN * P].reshape(-1, PIECES * OWN, P)
        shared = a[:, :, OWN * P:].reshape(-1, 1, P)
        return np.ascontiguousarray(np.concatenate([shared, own], axis=1).transpose(2, 0, 1))

    first = np.cumsum([0] + VOCABS[:-1]).astype(np.int32)
    w1 = x["W_top1"]
    pair_row = {pair: r for r, pair in enumerate(zip(*np.triu_indices(V, k=1)))}
    w1_pairs = np.zeros((P, SLOTS, H1), w1.dtype)
    for m in range(1, V):
        for n in range(m):
            r = pair_row[(0, n + 1)] if m == F else pair_row[(n + 1, m + 1)]
            w1_pairs[QUAD * ((m - 1) % 4) + n, (m - 1) // 4] = w1[r]
    n_pairs = V * F // 2
    arrays = {
        "table": np.concatenate([x[f"tbl_{f}"] for f in range(F)]),
        "ids": chunked(x["ids"]),
        "row_base": chunked(np.tile(first, (HALF, 1)))[:, 0, :],
        "dense_t": np.ascontiguousarray(x["r_dense"].T),
        "w1_pairs": w1_pairs,
        "w1_dense": np.ascontiguousarray(w1[n_pairs:]),
        "b1": np.ascontiguousarray(x["b_top1"].reshape(N1, P).T),
        "w2": np.ascontiguousarray(x["W_top2"].reshape(N1, P, H2).transpose(1, 0, 2)),
        "b2": np.ascontiguousarray(x["b_top2"].reshape(N2, P).T),
        "w3": np.ascontiguousarray(x["W_top3"].reshape(N2, P).T),
    }
    nc = bacc.Bacc("TRN2", target_bir_lowering=False, num_devices=1)
    aps = [nc.dram_tensor(name, a.shape, mybir.dt.from_np(a.dtype), kind="ExternalInput").ap()
           for name, a in arrays.items()]
    y = nc.dram_tensor("y", (1, B), mybir.dt.float32, kind="ExternalOutput").ap()
    program(nc, *aps, y)
    r = run_bass_kernel_spmd(nc, [arrays], core_ids=[0])
    return r.results[0]["y"].reshape(B, 1)
```

```python
from contextlib import ExitStack

import concourse.bass as bass
from concourse import mybir

VOCABS = [1250, 125000, 1250, 1250, 1000, 1250, 1250, 1000, 1000, 1250, 1250, 1000, 1000, 12500, 1250, 1000,
          1250, 1250, 1250, 12500, 1000, 1000, 1000, 12500, 1250, 1000]
P = 128
B = 512
F = len(VOCABS)
HOT = [4, 7]
GATHERED = [f for f in range(F) if f not in HOT]
NH, NG = len(HOT), len(GATHERED)
V = F + 1
KH = 8
HP = VOCABS[HOT[0]] // KH
HALF = 64
TILE = 2 * HALF
TILES = B // TILE
CHUNKS = HALF * NG // P
PIECES = 4
PS = HALF // PIECES
PC = PS * NG // P
GROUP = 4
GROUPS = PS // GROUP
QUAD = 32
SLOTS = (F + 3) // 4
H1, H2 = 512, 256
N1, N2 = H1 // P, H2 // P
BANK = 512


def program(nc, table, ids, row_base, dense_t, hot_table, hot_ids, hot_rows, w1_pairs, w1_dense, b1, w2, b2, w3, y):
    f32, i32, u32 = mybir.dt.float32, mybir.dt.int32, mybir.dt.uint32
    ALU = mybir.AluOpType
    ACT = mybir.ActivationFunctionType

    with ExitStack() as ctx:
        def sb(name, shape, dt=f32):
            return ctx.enter_context(nc.sbuf_tensor(name, shape, dt))

        def ps(name, shape):
            return ctx.enter_context(nc.psum_tensor(name, shape, f32))

        def sem(name):
            return ctx.enter_context(nc.semaphore(name))

        ids_sb = sb("ids_sb", [P, B // HALF, CHUNKS], i32)
        base_sb = sb("base_sb", [P, CHUNKS], i32)
        all_rows = sb("all_rows", [P, B // HALF, CHUNKS], i32)
        rows = sb("rows", [P, 2, CHUNKS], i32)
        gathered = sb("gathered", [P, 2, CHUNKS, P])
        ident = sb("ident", [P, P])
        hot_sb = sb("hot_sb", [HP, NH, KH, P])
        hot_ids_sb = sb("hot_ids_sb", [HP, NH, B], i32)
        hot_rows_sb = sb("hot_rows_sb", [HP, KH])
        onehot = sb("onehot", [HP, NH, KH, B])
        dense_sb = sb("dense_sb", [P, B])
        vecs = sb("vecs", [P, 2, HALF, QUAD])
        pairs = sb("pairs", [P, SLOTS, TILE])
        w1p_sb = sb("w1p_sb", [P, SLOTS, H1])
        w1d_sb = sb("w1d_sb", [P, H1])
        b1_sb = sb("b1_sb", [P, N1])
        w2_sb = sb("w2_sb", [P, N1, H2])
        b2_sb = sb("b2_sb", [P, N2])
        w3_sb = sb("w3_sb", [P, N2])
        h1_sb = sb("h1_sb", [P, N1, TILE])
        h2_sb = sb("h2_sb", [P, N2, TILE])
        y_sb = sb("y_sb", [1, B])

        turned = ps("turned", [P, PIECES, BANK])
        dots = ps("dots", [P, 2, GROUPS, P])
        spare = ps("spare", [P, 2, BANK])
        h1_ps = [spare[:, 0, 0:TILE], spare[:, 0, TILE:2 * TILE], spare[:, 1, 0:TILE], turned[:, 3, 0:TILE]]
        h2_ps = turned[:, 0:N2, 0:TILE]
        y_ps = turned[0:1, N2, 0:TILE]
        found = spare[:, 0, 0:NH * TILE].rearrange("p (f s) -> p f s", f=NH)

        ids_in = sem("ids_in")
        base_in = sem("base_in")
        dense_in = sem("dense_in")
        hot_in = sem("hot_in")
        hot_ids_in = sem("hot_ids_in")
        w1_in = sem("w1_in")
        w2_in = sem("w2_in")
        ident_zero = sem("ident_zero")
        ident_ready = sem("ident_ready")
        rows_found = sem("rows_found")
        half_begun = sem("half_begun")
        rows_ready = sem("rows_ready")
        landed = [sem(f"landed{c}") for c in range(2 * CHUNKS)]
        onehot_ready = sem("onehot_ready")
        found_ready = sem("found_ready")
        turned_ready = sem("turned_ready")
        vecs_dve = sem("vecs_dve")
        vecs_act = sem("vecs_act")
        dense_cols = sem("dense_cols")
        hot_cols = sem("hot_cols")
        dots_ready = sem("dots_ready")
        vecs_zero = sem("vecs_zero")
        pairs_dve = sem("pairs_dve")
        pairs_act = sem("pairs_act")
        h1_low = sem("h1_low")
        h1_mid = sem("h1_mid")
        pairs_free = sem("pairs_free")
        h1_dve = sem("h1_dve")
        h1_act = sem("h1_act")
        h2_sum = sem("h2_sum")
        h2_dve = sem("h2_dve")
        h2_act = sem("h2_act")
        y_sum = sem("y_sum")
        y_ready = sem("y_ready")
        stored = sem("stored")

        def evacuate(copy, half, k):
            src = turned[:, k, 0:PS * NG].rearrange("p (s f) -> p s f", f=NG)
            return copy(vecs[:, half, k * PS:(k + 1) * PS, 0:NG], src)

        def spread(copy, half, k, quads):
            for j in quads:
                for q in range(4):
                    n = (F - q + 3) // 4
                    s0 = half * HALF + k * PS + j
                    cols = dots[QUAD * j:QUAD * j + F, k % 2, :, V * j + 1 + q:V * j + 1 + q + 4 * (n - 1) + 1:4]
                    dst = pairs[QUAD * q:QUAD * q + F, 0:n, s0:s0 + PS - GROUP + 1:GROUP]
                    last = copy(dst, cols.rearrange("p g t -> p t g"))
            return last

        block = ctx.enter_context(nc.Block())

        @block.sync
        def _(sp):
            sp.dma_start(ids_sb[:, :], ids).then_inc(ids_in, 16)
            sp.dma_start(hot_sb[:, :, :, :], hot_table).then_inc(hot_in, 16)
            sp.dma_start(dense_sb[:, :], dense_t).then_inc(dense_in, 16)
            sp.dma_start(w1p_sb[:, :, :], w1_pairs).then_inc(w1_in, 16)
            sp.dma_start(w1d_sb[:, :], w1_dense).then_inc(w1_in, 16)
            sp.dma_start(w2_sb[:, :, :], w2).then_inc(w2_in, 16)
            sp.wait_ge(y_ready, TILES)
            sp.dma_start(y, y_sb[:, :]).then_inc(stored, 16)
            sp.wait_ge(stored, 16)

        @block.gpsimd
        def _(pool):
            nc.gpsimd.memset(ident[:, :], 0.0).then_inc(ident_zero, 1)
            pool.wait_ge(ident_zero, 1)
            nc.gpsimd.affine_select(out=ident[:, :], in_=ident[:, :], compare_op=ALU.not_equal, fill=1.0,
                                    base=0, pattern=[[-1, P]], channel_multiplier=1).then_inc(ident_ready, 1)
            with pool.Fori(0, TILES) as t:
                for half in range(2):
                    pool.wait_ge(rows_ready, 2 * t + half + 1)
                    pool.sem_inc(half_begun, 1)
                    for c in range(CHUNKS):
                        nc.gpsimd.indirect_dma_start(
                            gathered[:, half, c, :], None, table,
                            bass.IndirectOffsetOnAxis(rows[:, half, c:c + 1].bitcast(u32), 0),
                        ).then_inc(landed[half * CHUNKS + c], 16)

        @block.tensor
        def _(pe):
            def transposes(t, half, k):
                for i in range(PC):
                    c = k * PC + i
                    pe.wait_ge(landed[half * CHUNKS + c], 16 * t + 16)
                    last = nc.tensor.transpose(turned[:, k, i * P:(i + 1) * P], gathered[:, half, c, :], ident[:, :])
                last.then_inc(turned_ready, 1)

            def dot_products(t, half, k):
                n = 8 * t + 4 * half + k
                pe.wait_ge((vecs_dve, vecs_act)[k % 2], 4 * t + 2 * half + k // 2 + 1)
                if 4 * half + k >= 2:
                    pe.wait_ge(pairs_dve, n - 1)
                    pe.wait_ge(pairs_act, n - 1)
                for g in range(GROUPS):
                    at = k * PS + g * GROUP
                    group = vecs[:, half, at:at + GROUP, :]
                    last = nc.tensor.matmul(dots[:, k % 2, g, 0:GROUP * V], group.rearrange("p s v -> p (s v)"),
                                            group[:, :, 0:V], start=True, stop=True)
                last.then_inc(dots_ready, 1)

            def one_hot_lookups(t):
                for f in range(NH):
                    for k in range(KH):
                        last = nc.tensor.matmul(found[:, f, :], hot_sb[:, f, k, :],
                                                onehot[:, f, k, bass.ds(t * TILE, TILE)],
                                                start=k == 0, stop=k == KH - 1)
                last.then_inc(found_ready, 1)

            def mlp(t):
                dense = vecs[:, :, :, F].rearrange("p h s -> p (h s)")

                def dense_share(i):
                    nc.tensor.matmul(h1_ps[i], w1d_sb[:, i * P:(i + 1) * P], dense, start=True, stop=False)

                for i in (0, 2, 3):
                    dense_share(i)
                pe.wait_ge(pairs_dve, 8 * t + 8)
                pe.wait_ge(pairs_act, 8 * t + 8)
                for i in range(N1):
                    if i == 1:
                        dense_share(i)
                    for s in range(SLOTS):
                        last = nc.tensor.matmul(h1_ps[i], w1p_sb[:, s, i * P:(i + 1) * P], pairs[:, s, :],
                                                start=False, stop=s == SLOTS - 1)
                    if i:
                        last.then_inc((h1_low, h1_mid, pairs_free)[i - 1], 1)
                for i in range(N1):
                    if i == 0:
                        pe.wait_ge(h1_dve, 2 * t + 1)
                    if i == 2:
                        pe.wait_ge(h1_dve, 2 * t + 2)
                    if i == 3:
                        pe.wait_ge(h1_act, t + 1)
                    for o in range(N2):
                        last = nc.tensor.matmul(h2_ps[:, o, :], w2_sb[:, i, o * P:(o + 1) * P],
                                                h1_sb[:, i, :], start=i == 0, stop=i == N1 - 1)
                        if i == N1 - 1:
                            last.then_inc(h2_sum, 1)
                pe.wait_ge(h2_dve, t + 1)
                pe.wait_ge(h2_act, t + 1)
                for o in range(N2):
                    last = nc.tensor.matmul(y_ps, w3_sb[:, o:o + 1], h2_sb[:, o, :],
                                            start=o == 0, stop=o == N2 - 1)
                last.then_inc(y_sum, 1)

            def tile(t):
                one_hot_lookups(t)
                half_tile(t, 0)
                half_tile(t, 1)
                mlp(t)

            def half_tile(t, half):
                transposes(t, half, 0)
                for k in range(1, PIECES):
                    transposes(t, half, k)
                    if k == 1 and half == 0:
                        pe.wait_ge(dense_cols, t + 1)
                        pe.wait_ge(hot_cols, t + 1)
                    dot_products(t, half, k - 1)
                dot_products(t, half, PIECES - 1)

            pe.wait_ge(ident_ready, 1)
            pe.wait_ge(vecs_zero, 1)
            pe.wait_ge(hot_in, 16)
            pe.wait_ge(onehot_ready, 1)
            one_hot_lookups(0)
            half_tile(0, 0)
            half_tile(0, 1)
            pe.wait_ge(w1_in, 32)
            pe.wait_ge(w2_in, 64)
            mlp(0)
            with pe.Fori(1, TILES) as t:
                pe.wait_ge(y_ready, t)
                tile(t)

        @block.vector
        def _(dve):
            copy = nc.vector.tensor_copy

            def place_rows(t, half):
                copy(rows[:, half, :], all_rows[:, bass.ds(2 * t + half, 1), :].rearrange("p a c -> p (a c)")
                     ).then_inc(rows_ready, 1)

            def half_tile(t, half):
                def vectors(k):
                    dve.wait_ge(turned_ready, 8 * t + 4 * half + k + 1)
                    evacuate(copy, half, k).then_inc(vecs_dve, 1)

                def products(k):
                    dve.wait_ge(dots_ready, 8 * t + 4 * half + k + 1)
                    spread(copy, half, k, (0, 1)).then_inc(pairs_dve, 1)

                vectors(0)
                if half == 0:
                    dve.wait_ge(pairs_free, t + 1)
                products(0)
                vectors(2)
                products(1)
                products(2)
                products(PIECES - 1)

            def mlp(t):
                def relu(i):
                    return nc.vector.tensor_scalar(h1_sb[:, i, :], h1_ps[i], b1_sb[:, i:i + 1], 0.0,
                                                   ALU.add, ALU.max)

                dve.wait_ge(h1_low, t + 1)
                relu(0)
                relu(1).then_inc(h1_dve, 1)
                dve.wait_ge(h1_mid, t + 1)
                relu(2).then_inc(h1_dve, 1)
                dve.wait_ge(h2_sum, N2 * t + 1)
                nc.vector.tensor_scalar(h2_sb[:, 0, :], h2_ps[:, 0, :], b2_sb[:, 0:1], 0.0,
                                        ALU.add, ALU.max).then_inc(h2_dve, 1)
                dve.wait_ge(y_sum, t + 1)
                copy(y_sb[0:1, bass.ds(t * TILE, TILE)], y_ps).then_inc(y_ready, 1)

            dve.wait_ge(ids_in, 16)
            dve.wait_ge(base_in, 16)
            base_all = base_sb[:, :].unsqueeze(1).to_broadcast([P, B // HALF, CHUNKS])
            nc.vector.tensor_tensor(all_rows[:, :, :], ids_sb[:, :, :], base_all, ALU.add).then_inc(rows_found, 1)
            dve.wait_ge(rows_found, 1)
            place_rows(0, 0)
            place_rows(0, 1)
            nc.vector.memset(vecs[:, :, :, :], 0.0).then_inc(vecs_zero, 1)
            nc.vector.memset(pairs[:, :, :], 0.0).then_inc(pairs_free, 1)
            dve.wait_ge(hot_ids_in, 32)
            for f in range(NH):
                for k in range(KH):
                    last = nc.vector.tensor_scalar(onehot[:, f, k, :], hot_ids_sb[:, f, :], hot_rows_sb[:, k:k + 1],
                                                   None, ALU.is_equal)
            last.then_inc(onehot_ready, 1)
            dve.wait_ge(vecs_zero, 1)
            dve.wait_ge(w2_in, 64)
            with dve.Fori(0, TILES - 1) as t:
                for half in range(2):
                    half_tile(t, half)
                    place_rows(t + 1, half)
                mlp(t)
            half_tile(TILES - 1, 0)
            half_tile(TILES - 1, 1)
            mlp(TILES - 1)

        @block.scalar
        def _(act):
            def copy(dst, src):
                return nc.scalar.activation(dst, src, ACT.Copy)

            act.dma_start(base_sb[:, :], row_base).then_inc(base_in, 16)
            act.dma_start(hot_ids_sb[:, :, :], hot_ids.unsqueeze(0).to_broadcast([HP, NH, B])
                          ).then_inc(hot_ids_in, 16)
            act.dma_start(hot_rows_sb[:, :], hot_rows).then_inc(hot_ids_in, 16)
            act.dma_start(b1_sb[:, :], b1).then_inc(w2_in, 16)
            act.dma_start(b2_sb[:, :], b2).then_inc(w2_in, 16)
            act.dma_start(w3_sb[:, :], w3).then_inc(w2_in, 16)

            def half_tile(t, half):
                def vectors(k):
                    act.wait_ge(turned_ready, 8 * t + 4 * half + k + 1)
                    evacuate(copy, half, k).then_inc(vecs_act, 1)

                def products(k):
                    act.wait_ge(dots_ready, 8 * t + 4 * half + k + 1)
                    spread(copy, half, k, (2, 3)).then_inc(pairs_act, 1)

                if half == 0:
                    act.wait_ge(pairs_free, t + 1)
                    src = dense_sb[:, bass.ds(t * TILE, TILE)].rearrange("p (h s) -> p h s", h=2)
                    copy(vecs[:, :, :, F], src).then_inc(dense_cols, 1)
                    act.wait_ge(found_ready, t + 1)
                    copy(vecs[:, :, :, NG:F].rearrange("p h s v -> p v (h s)"), found).then_inc(hot_cols, 1)
                vectors(1)
                products(0)
                products(1)
                vectors(3)
                products(2)
                products(PIECES - 1)

            def mlp(t):
                act.wait_ge(pairs_free, t + 2)
                nc.scalar.activation(h1_sb[:, 3, :], h1_ps[3], ACT.Relu, bias=b1_sb[:, 3:4]).then_inc(h1_act, 1)
                act.wait_ge(h2_sum, N2 * t + 2)
                nc.scalar.activation(h2_sb[:, 1, :], h2_ps[:, 1, :], ACT.Relu,
                                     bias=b2_sb[:, 1:2]).then_inc(h2_act, 1)

            act.wait_ge(dense_in, 16)
            act.wait_ge(vecs_zero, 1)
            act.wait_ge(w2_in, 64)
            with act.Fori(0, TILES) as t:
                half_tile(t, 0)
                half_tile(t, 1)
                mlp(t)


def kernel(**inputs):
    import numpy as np
    import concourse.bacc as bacc
    from concourse.bass_utils import run_bass_kernel_spmd

    x = {name: np.asarray(a) for name, a in inputs.items()}

    def chunked(a):
        return np.ascontiguousarray(a.reshape(-1, CHUNKS, P).transpose(2, 0, 1))

    first = np.cumsum([0] + [VOCABS[f] for f in GATHERED[:-1]]).astype(np.int32)
    w1 = x["W_top1"]
    ref_number = [f + 1 for f in GATHERED + HOT] + [0]
    pair_row = {pair: r for r, pair in enumerate(zip(*np.triu_indices(V, k=1)))}
    w1_pairs = np.zeros((P, SLOTS, H1), w1.dtype)
    for m in range(1, V):
        for n in range(m):
            r = pair_row[tuple(sorted((ref_number[n], ref_number[m])))]
            w1_pairs[QUAD * ((m - 1) % 4) + n, (m - 1) // 4] = w1[r]
    n_pairs = V * F // 2
    arrays = {
        "table": np.concatenate([x[f"tbl_{f}"] for f in GATHERED]),
        "ids": chunked(x["ids"][:, GATHERED]),
        "row_base": chunked(np.tile(first, (HALF, 1)))[:, 0, :],
        "dense_t": np.ascontiguousarray(x["r_dense"].T),
        "hot_table": np.ascontiguousarray(
            np.stack([x[f"tbl_{f}"].reshape(HP, KH, P) for f in HOT], axis=1)),
        "hot_ids": np.ascontiguousarray(x["ids"][:, HOT].T),
        "hot_rows": np.arange(HP * KH, dtype=np.float32).reshape(HP, KH),
        "w1_pairs": w1_pairs,
        "w1_dense": np.ascontiguousarray(w1[n_pairs:]),
        "b1": np.ascontiguousarray(x["b_top1"].reshape(N1, P).T),
        "w2": np.ascontiguousarray(x["W_top2"].reshape(N1, P, H2).transpose(1, 0, 2)),
        "b2": np.ascontiguousarray(x["b_top2"].reshape(N2, P).T),
        "w3": np.ascontiguousarray(x["W_top3"].reshape(N2, P).T),
    }
    nc = bacc.Bacc("TRN2", target_bir_lowering=False, num_devices=1)
    aps = [nc.dram_tensor(name, a.shape, mybir.dt.from_np(a.dtype), kind="ExternalInput").ap()
           for name, a in arrays.items()]
    y = nc.dram_tensor("y", (1, B), mybir.dt.float32, kind="ExternalOutput").ap()
    program(nc, *aps, y)
    r = run_bass_kernel_spmd(nc, [arrays], core_ids=[0])
    return r.results[0]["y"].reshape(B, 1)
```

```python
from contextlib import ExitStack

import concourse.bass as bass
from concourse import mybir

VOCABS = [1250, 125000, 1250, 1250, 1000, 1250, 1250, 1000, 1000, 1250, 1250, 1000, 1000, 12500, 1250, 1000,
          1250, 1250, 1250, 12500, 1000, 1000, 1000, 12500, 1250, 1000]
P = 128
B = 512
F = len(VOCABS)
HOT = [4, 7, 8, 11]
GATHERED = [f for f in range(F) if f not in HOT]
NH, NG = len(HOT), len(GATHERED)
V = F + 1
KH = 8
HP = VOCABS[HOT[0]] // KH
KD = 6
HALF = 64
TILE = 2 * HALF
TILES = B // TILE
HALVES = B // HALF
CHUNKS = HALF * NG // P
PIECES = 4
PS = HALF // PIECES
GROUP = 4
GROUPS = PS // GROUP
LAST_EARLY = 2 * GROUP
QUAD = 32
LOW = 3
SLOTS = (V - LOW) // 4
DENSE = NH
COPIES = 2
H1, H2 = 512, 256
N1, N2 = H1 // P, H2 // P
BANK = 512


def program(nc, table, ids_and_base, dense_t, hot_table, hot_ids, hot_rows, w1_pairs, w1_dense, b1, w2, b2, w3, y):
    f32, f32r, i32, u32 = mybir.dt.float32, mybir.dt.float32r, mybir.dt.int32, mybir.dt.uint32
    ALU = mybir.AluOpType
    ACT = mybir.ActivationFunctionType

    with ExitStack() as ctx:
        def sb(name, shape, dt=f32):
            return ctx.enter_context(nc.sbuf_tensor(name, shape, dt))

        def ps(name, shape):
            return ctx.enter_context(nc.psum_tensor(name, shape, f32))

        def sem(name):
            return ctx.enter_context(nc.semaphore(name))

        ids_sb = sb("ids_sb", [P, HALVES + 1, CHUNKS], i32)
        all_rows = sb("all_rows", [P, HALVES, CHUNKS], i32)
        rows = sb("rows", [P, 2, CHUNKS], i32)
        gathered = sb("gathered", [P, 2, CHUNKS, P])
        ident = sb("ident", [P, P])
        hot_sb = sb("hot_sb", [HP, NH, KH, P])
        hot_high = sb("hot_high", [HP, NH, KH, P], f32r)
        hot_low = sb("hot_low", [HP, NH, KH, P], f32r)
        hot_ids_sb = sb("hot_ids_sb", [HP, NH, B], i32)
        hot_rows_sb = sb("hot_rows_sb", [HP, KH])
        onehot = sb("onehot", [HP, 2, KH, B], f32r)
        distance = sb("distance", [HP, KH - KD, B])
        extra = sb("extra", [P, NH + 1, B])
        vecs = sb("vecs", [P, 2, HALF, QUAD])
        pairs = sb("pairs", [P, SLOTS, TILE])
        w1p_sb = sb("w1p_sb", [P, SLOTS, H1])
        w1d_sb = sb("w1d_sb", [P, H1])
        b1_sb = sb("b1_sb", [P, N1])
        w2_sb = sb("w2_sb", [P, N1, H2])
        b2_sb = sb("b2_sb", [P, N2])
        w3_sb = sb("w3_sb", [P, N2])
        h1_sb = sb("h1_sb", [P, N1, TILE])
        h2_sb = sb("h2_sb", [P, N2, TILE])
        y_sb = sb("y_sb", [1, B])

        turned = ps("turned", [P, PIECES, BANK])
        dots = ps("dots", [P, 2, GROUPS, P])
        spare = ps("spare", [P, 2, BANK])
        h1_ps = [spare[:, 0, 0:TILE], turned[:, PIECES - 1, 0:TILE], spare[:, 1, 0:TILE], dots[:, 0, 0, :]]
        h2_ps = [spare[:, o, 2 * TILE:3 * TILE] for o in range(N2)]
        y_ps = spare[0:1, 0, 3 * TILE:4 * TILE]
        hot_ids_ps = [dots[0:HP, i, :, :].rearrange("p g c -> p (g c)") for i in range(2)]

        ids_in = sem("ids_in")
        dense_in = sem("dense_in")
        hot_in = [sem(f"hot_in{f}") for f in range(NH)]
        hot_ids_in = [sem(f"hot_ids_in{f}") for f in range(NH)]
        hot_rows_in = sem("hot_rows_in")
        w1_in = sem("w1_in")
        w2_in = sem("w2_in")
        small_in = sem("small_in")
        ident_zero = sem("ident_zero")
        ident_ready = sem("ident_ready")
        half_begun = sem("half_begun")
        rows_found = sem("rows_found")
        rows_ready = sem("rows_ready")
        landed = [sem(f"landed{c}") for c in range(2 * CHUNKS)]
        first_ids_ready = sem("first_ids_ready")
        ids_ready = sem("ids_ready")
        high_ready = sem("high_ready")
        low_ready = sem("low_ready")
        onehot_dve = sem("onehot_dve")
        distance_ready = sem("distance_ready")
        onehot_act = sem("onehot_act")
        found_ready = sem("found_ready")
        found_out = sem("found_out")
        turned_ready = sem("turned_ready")
        vecs_dve = sem("vecs_dve")
        vecs_act = sem("vecs_act")
        last_turned = sem("last_turned")
        last_vecs = sem("last_vecs")
        extra_cols = sem("extra_cols")
        dots_ready = sem("dots_ready")
        pad_zero = sem("pad_zero")
        pairs_dve = sem("pairs_dve")
        pairs_act = sem("pairs_act")
        spread_dve = sem("spread_dve")
        spread_act = sem("spread_act")
        h1_low = sem("h1_low")
        h1_mid = sem("h1_mid")
        pairs_free = sem("pairs_free")
        h1_dve = sem("h1_dve")
        h1_act = sem("h1_act")
        h2_sum = sem("h2_sum")
        h2_dve = sem("h2_dve")
        h2_act = sem("h2_act")
        y_sum = sem("y_sum")
        y_out = sem("y_out")
        stored = sem("stored")

        def piece_parts(k):
            lo, hi = k * PS * NG, (k + 1) * PS * NG
            whole, some = [], []
            for c in range(lo // P, -(-hi // P)):
                a, b = max(lo - c * P, 0), min(hi - c * P, P)
                if (a, b) == (0, P):
                    whole.append((c, a, b, c * P - lo))
                    continue
                if a == QUAD and b > 2 * QUAD:
                    some.append((c, a, 2 * QUAD, c * P + a - lo))
                    a = 2 * QUAD
                some.append((c, a, b, c * P + a - lo))
            return whole, some


        def evacuate(copy, m, lo=0, hi=PS, bank=None):
            half, k = divmod(m, PIECES)
            src = turned[:, k if bank is None else bank, lo * NG:hi * NG].rearrange("p (s f) -> p s f", f=NG)
            return copy(vecs[:, half, k * PS + lo:k * PS + hi, NH + 1:V], src)

        def spread(engine, copy, t, m, quads, spread_low, done):
            def samples(j):
                return slice(m * PS + j, m * PS + j + PS - GROUP + 1, GROUP)

            for q in range(4):
                for j in quads:
                    col = V * j + LOW + q
                    cols = dots[QUAD * j:QUAD * j + V + COPIES, m % 2, :, col:col + 4 * (SLOTS - 1) + 1:4]
                    dst = pairs[QUAD * q:QUAD * q + V + COPIES, :, samples(j)]
                    last = copy(dst, cols.rearrange("p g t -> p t g"))
                if q == 0:
                    last.then_inc(spread_low, 1)
            engine.wait_ge(spread_low, 8 * t + m + 1)
            for j in quads:
                cols = dots[QUAD * j:QUAD * j + 2, m % 2, :, V * j + 1:V * j + 3]
                last = copy(pairs[0:2, 0:2, samples(j)], cols.rearrange("p g t -> p t g"))
            last.then_inc(done, 1)

        block = ctx.enter_context(nc.Block())

        @block.sync
        def _(sp):
            def hot_ids_load(f):
                sp.dma_start(hot_ids_sb[:, f, :], hot_ids[f:f + 1, :].to_broadcast([HP, B])
                             ).then_inc(hot_ids_in[f], 16)

            sp.dma_start(ids_sb[:, :, :], ids_and_base).then_inc(ids_in, 16)
            sp.dma_start(hot_rows_sb[:, :], hot_rows).then_inc(hot_rows_in, 16)
            for f in range(NH):
                sp.dma_start(hot_sb[:, f, :, :], hot_table[:, f, :, :]).then_inc(hot_in[f], 16)
                if f + 1 < NH:
                    hot_ids_load(f + 1)
            sp.dma_start(extra[:, DENSE, :], dense_t).then_inc(dense_in, 16)
            sp.dma_start(b1_sb[:, :], b1).then_inc(small_in, 16)
            sp.dma_start(b2_sb[:, :], b2).then_inc(small_in, 16)
            sp.dma_start(w3_sb[:, :], w3).then_inc(small_in, 16)
            sp.wait_ge(rows_found, 1)
            for h in range(2, HALVES):
                for c in range(CHUNKS):
                    sp.wait_ge(landed[h % 2 * CHUNKS + c], h // 2 * 16)
                sp.wait_ge(rows_ready, 16 * (h - 1))
                sp.dma_start(rows[:, h % 2, :], all_rows[:, h, :]).then_inc(rows_ready, 16)
                if h == 2:
                    sp.dma_start(w1p_sb[:, :, :], w1_pairs).then_inc(w1_in, 16)
                    sp.dma_start(w1d_sb[:, :], w1_dense).then_inc(w1_in, 16)
                    sp.dma_start(w2_sb[:, :, :], w2).then_inc(w2_in, 16)
            sp.wait_ge(y_out, TILES + 1)
            sp.dma_start(y, y_sb[:, :]).then_inc(stored, 16)
            sp.wait_ge(stored, 16)

        @block.gpsimd
        def _(pool):
            nc.gpsimd.memset(ident[:, :], 0.0).then_inc(ident_zero, 1)
            pool.wait_ge(ident_zero, 1)
            nc.gpsimd.affine_select(out=ident[:, :], in_=ident[:, :], compare_op=ALU.not_equal, fill=1.0,
                                    base=0, pattern=[[-1, P]], channel_multiplier=1).then_inc(ident_ready, 1)
            nc.gpsimd.memset(vecs[:, :, :, V + COPIES:QUAD], 0.0).then_inc(pad_zero, 1)
            nc.gpsimd.memset(pairs[:, :, :], 0.0).then_inc(pairs_free, 1)

            def gather(half):
                for c in range(CHUNKS):
                    nc.gpsimd.indirect_dma_start(
                        gathered[:, half, c, :], None, table,
                        bass.IndirectOffsetOnAxis(rows[:, half, c:c + 1].bitcast(u32), 0),
                    ).then_inc(landed[half * CHUNKS + c], 16)

            pool.wait_ge(rows_ready, 16)
            gather(0)
            gather(1)
            with pool.Fori(1, TILES) as t:
                for half in range(2):
                    pool.wait_ge(rows_ready, 32 * t + 16 * half)
                    pool.wait_ge(turned_ready, 8 * t - 4 + 4 * half)
                    pool.sem_inc(half_begun, 1)
                    gather(half)

        @block.tensor
        def _(pe):
            def look_up(f):
                if f >= 2:
                    pe.wait_ge(found_out, f - 1)
                for part in (hot_high, hot_low):
                    if part is hot_high:
                        pe.wait_ge(high_ready, f + 1)
                    else:
                        pe.wait_ge(low_ready, f + 1)
                    for k in range(KH):
                        if part is hot_high and k in (0, KD // 2):
                            pe.wait_ge(onehot_dve, 2 * f + (1 if k == 0 else 2))
                        if part is hot_high and k >= KD:
                            pe.wait_ge(onehot_act, (KH - KD) * f + k - KD + 1)
                        last = nc.tensor.matmul(spare[:, f % 2, :], part[:, f, k, :], onehot[:, f % 2, k, :],
                                                start=k == 0 and part is hot_high,
                                                stop=k == KH - 1 and part is hot_low)
                last.then_inc(found_ready, 1)

            def turn(half, bank, c, a, b, col):
                return nc.tensor.transpose(turned[:, bank, col:col + b - a], gathered[a:b, half, c, :],
                                           ident[a:b, a:b])

            def transposes(t, m):
                half, k = divmod(m, PIECES)
                whole, some = piece_parts(k)
                for part in some[:1] + some[-1:] + whole:
                    pe.wait_ge(landed[half * CHUNKS + part[0]], 16 * t + 16)
                    if part in whole:
                        turn(half, k, *part)
                for part in some:
                    last = turn(half, k, *part)
                last.then_inc(turned_ready, 1)

            def group_products(m, groups):
                half, k = divmod(m, PIECES)
                for g in groups:
                    at = k * PS + g * GROUP
                    group = vecs[:, half, at:at + GROUP, :]
                    last = nc.tensor.matmul(dots[:, m % 2, g, 0:GROUP * V], group.rearrange("p s v -> p (s v)"),
                                            group[:, :, 0:V], start=True, stop=True)
                return last

            def dot_products(t, m):
                half, k = divmod(m, PIECES)
                pe.wait_ge((vecs_dve, vecs_act)[half], 4 * t + k + 1)
                if m >= 2:
                    pe.wait_ge(pairs_dve, 8 * t + m - 1)
                    pe.wait_ge(pairs_act, 8 * t + m - 1)
                group_products(m, range(GROUPS)).then_inc(dots_ready, 1)

            def dense_share(t, i):
                nc.tensor.matmul(h1_ps[i], w1d_sb[:, i * P:(i + 1) * P],
                                 extra[:, DENSE, bass.ds(t * TILE, TILE)], start=True, stop=False)

            def begin_mlp(t):
                pe.wait_ge(found_out, NH)
                pe.wait_ge(y_out, t + 1)
                pe.wait_ge(w1_in, 32)
                dense_share(t, 0)
                dense_share(t, 2)

            def mlp(t, last_tile=False):
                def second_layer(o, i):
                    return nc.tensor.matmul(h2_ps[o], w2_sb[:, i, o * P:(o + 1) * P], h1_sb[:, i, :],
                                            start=i == 0, stop=i == N1 - 1)

                pe.wait_ge(pairs_dve, 8 * t + 7)
                pe.wait_ge(pairs_act, 8 * t + 7)
                dense_share(t, 3)
                dense_share(t, 1)
                if not last_tile:
                    transposes(t + 1, 0)
                pe.wait_ge(pairs_dve, 8 * t + 8)
                pe.wait_ge(pairs_act, 8 * t + 8)
                for i in range(N1):
                    for s in range(SLOTS):
                        last = nc.tensor.matmul(h1_ps[i], w1p_sb[:, s, i * P:(i + 1) * P], pairs[:, s, :],
                                                start=False, stop=s == SLOTS - 1)
                    if i:
                        last.then_inc((h1_low, h1_mid, pairs_free)[i - 1], 1)
                if not last_tile:
                    transposes(t + 1, 1)
                pe.wait_ge(w2_in, 16)
                pe.wait_ge(h1_dve, 2 * t + 1)
                second_layer(0, 0)
                second_layer(0, 1)
                pe.wait_ge(h1_act, t + 1)
                second_layer(0, 2)
                second_layer(1, 0)
                second_layer(1, 1)
                pe.wait_ge(h1_dve, 2 * t + 2)
                second_layer(0, 3).then_inc(h2_sum, 1)
                second_layer(1, 2)
                second_layer(1, 3).then_inc(h2_sum, 1)
                if not last_tile:
                    transposes(t + 1, 2)
                pe.wait_ge(h2_act, t + 1)
                nc.tensor.matmul(y_ps, w3_sb[:, 0:1], h2_sb[:, 0, :], start=True, stop=False)
                pe.wait_ge(h2_dve, t + 1)
                nc.tensor.matmul(y_ps, w3_sb[:, 1:2], h2_sb[:, 1, :], start=False, stop=True).then_inc(y_sum, 1)

            pe.wait_ge(ident_ready, 1)
            look_up(0)
            look_up(1)
            transposes(0, 0)
            transposes(0, 1)
            look_up(2)
            transposes(0, 2)
            transposes(0, 3)
            look_up(3)
            pe.wait_ge(pad_zero, 1)
            pe.wait_ge(small_in, 48)
            with pe.Fori(0, TILES - 1) as t:
                pe.wait_ge(vecs_dve, 4 * t + 1)
                transposes(t, 4)
                pe.wait_ge(extra_cols, t + 1)
                dot_products(t, 0)
                dot_products(t, 1)
                transposes(t, 5)
                dot_products(t, 2)
                dot_products(t, 3)
                transposes(t, 6)
                dot_products(t, 4)
                dot_products(t, 5)
                begin_mlp(t)
                transposes(t, 7)
                dot_products(t, 6)
                dot_products(t, 7)
                mlp(t)
                transposes(t + 1, 3)
            t = TILES - 1
            pe.wait_ge(extra_cols, t + 1)
            dot_products(t, 0)
            transposes(t, 4)
            dot_products(t, 1)
            dot_products(t, 2)
            transposes(t, 5)
            dot_products(t, 3)
            dot_products(t, 4)
            dot_products(t, 5)
            transposes(t, 6)
            begin_mlp(t)
            m, k = 7, PIECES - 1
            whole, some = piece_parts(k)
            for part in some + whole[:1]:
                pe.wait_ge(landed[CHUNKS + part[0]], 16 * TILES)
                last = turn(1, k, *part)
            last.then_inc(last_turned, 1)
            turn(1, 0, *whole[0])
            dot_products(t, 6)
            pe.wait_ge(landed[2 * CHUNKS - 1], 16 * TILES)
            turn(1, 0, *whole[1]).then_inc(turned_ready, 1)
            pe.wait_ge(pairs_dve, 8 * t + m - 1)
            pe.wait_ge(pairs_act, 8 * t + m - 1)
            pe.wait_ge(last_vecs, 1)
            group_products(m, range(LAST_EARLY // GROUP))
            pe.wait_ge(vecs_act, 4 * TILES)
            group_products(m, range(LAST_EARLY // GROUP, GROUPS)).then_inc(dots_ready, 1)
            mlp(t, last_tile=True)

        @block.vector
        def _(dve):
            copy = nc.vector.tensor_copy

            def vectors(t, m):
                dve.wait_ge(turned_ready, 8 * t + m + 1)
                evacuate(copy, m).then_inc(vecs_dve, 1)

            def products(t, m):
                dve.wait_ge(dots_ready, 8 * t + m + 1)
                spread(dve, copy, t, m, (0, 1), spread_dve, pairs_dve)

            def mlp(t, last_tile=False):
                if not last_tile:
                    vectors(t + 1, 0)
                dve.wait_ge(h1_low, t + 1)
                for i in (0, 1, 3):
                    if i == 3:
                        dve.wait_ge(pairs_free, t + 2)
                    last = nc.vector.tensor_scalar(h1_sb[:, i, :], h1_ps[i], b1_sb[:, i:i + 1], 0.0,
                                                   ALU.add, ALU.max)
                    if i:
                        last.then_inc(h1_dve, 1)
                if not last_tile:
                    vectors(t + 1, 1)
                dve.wait_ge(h2_sum, N2 * t + 2)
                nc.vector.tensor_scalar(h2_sb[:, 1, :], h2_ps[1], b2_sb[:, 1:2], 0.0,
                                        ALU.add, ALU.max).then_inc(h2_dve, 1)
                if not last_tile:
                    vectors(t + 1, 2)
                dve.wait_ge(y_sum, t + 1)
                copy(y_sb[0:1, bass.ds(t * TILE, TILE)], y_ps).then_inc(y_out, 1)
                if not last_tile:
                    vectors(t + 1, 3)

            def look_up(f):
                if f:
                    dve.wait_ge(ids_ready, f)
                else:
                    dve.wait_ge(first_ids_ready, 1)
                if f >= 2:
                    dve.wait_ge(found_ready, f - 1)
                n = KD // 2
                for k in (0, n):
                    nc.vector.tensor_tensor(
                        onehot[:, f % 2, k:k + n, :], hot_ids_ps[f % 2].unsqueeze(1).to_broadcast([HP, n, B]),
                        hot_rows_sb[:, k:k + n].unsqueeze(2).to_broadcast([HP, n, B]), ALU.is_equal,
                    ).then_inc(onehot_dve, 1)
                dve.wait_ge(high_ready, f + 1)
                nc.vector.tensor_tensor(hot_low[:, f, :, :], hot_sb[:, f, :, :], hot_high[:, f, :, :].bitcast(f32),
                                        ALU.subtract).then_inc(low_ready, 1)

            nc.vector.memset(y_sb[:, :], 0.0).then_inc(y_out, 1)
            dve.wait_ge(ids_in, 16)
            base_all = ids_sb[:, HALVES, :].unsqueeze(1).to_broadcast([P, HALVES, CHUNKS])
            nc.vector.tensor_tensor(rows[:, :, :], ids_sb[:, 0:2, :], base_all[:, 0:2, :],
                                    ALU.add).then_inc(rows_ready, 16)
            nc.vector.tensor_tensor(all_rows[:, :, :], ids_sb[:, 0:HALVES, :], base_all,
                                    ALU.add).then_inc(rows_found, 1)
            dve.wait_ge(hot_ids_in[0], 16)
            copy(hot_ids_ps[0], hot_ids_sb[:, 0, :]).then_inc(first_ids_ready, 1)
            dve.wait_ge(hot_rows_in, 16)
            for f in range(NH):
                look_up(f)
            for m in range(PIECES):
                vectors(0, m)
            dve.wait_ge(small_in, 48)
            with dve.Fori(0, TILES - 1) as t:
                dve.wait_ge(pairs_free, t + 1)
                for m in range(2 * PIECES):
                    products(t, m)
                mlp(t)
            t = TILES - 1
            dve.wait_ge(pairs_free, t + 1)
            for m in range(2 * PIECES):
                products(t, m)
            mlp(t, last_tile=True)

        @block.scalar
        def _(act):
            def copy(dst, src):
                return nc.scalar.activation(dst, src, ACT.Copy)

            def vectors(t, m):
                act.wait_ge(turned_ready, 8 * t + m + 1)
                evacuate(copy, m).then_inc(vecs_act, 1)

            def products(t, m):
                act.wait_ge(dots_ready, 8 * t + m + 1)
                spread(act, copy, t, m, (2, 3), spread_act, pairs_act)

            def place_columns(t, col, n, source):
                return copy(vecs[:, :, :, col:col + n].rearrange("p h s v -> p v (h s)"),
                            extra[:, source:source + n, bass.ds(t * TILE, TILE)])

            def not_gathered(t):
                place_columns(t, 0, NH + 1, 0)
                place_columns(t, V, COPIES, 0).then_inc(extra_cols, 1)

            def mlp(t):
                act.wait_ge(h1_mid, t + 1)
                nc.scalar.activation(h1_sb[:, 2, :], h1_ps[2], ACT.Relu, bias=b1_sb[:, 2:3]).then_inc(h1_act, 1)
                act.wait_ge(h2_sum, N2 * t + 1)
                nc.scalar.activation(h2_sb[:, 0, :], h2_ps[0], ACT.Relu, bias=b2_sb[:, 0:1]).then_inc(h2_act, 1)

            def split_table(f):
                act.wait_ge(hot_in[f], 16)
                copy(hot_high[:, f, :, :], hot_sb[:, f, :, :]).then_inc(high_ready, 1)

            def place_ids(f):
                act.wait_ge(hot_ids_in[f], 16)
                if f >= 2:
                    act.wait_ge(onehot_dve, 2 * (f - 1))
                copy(hot_ids_ps[f % 2], hot_ids_sb[:, f, :]).then_inc(ids_ready, 1)

            def one_hot(f):
                act.wait_ge(hot_ids_in[f], 16)
                act.wait_ge(hot_rows_in, 16)
                if f:
                    act.wait_ge(onehot_act, (KH - KD) * f)
                if f >= 2:
                    act.wait_ge(found_ready, f - 1)
                for k in range(KD, KH):
                    nc.scalar.activation(distance[:, k - KD, :], hot_ids_sb[:, f, :], ACT.Abs,
                                         bias=hot_rows_sb[:, k:k + 1], scale=-1.0).then_inc(distance_ready, 1)
                for k in range(KD, KH):
                    act.wait_ge(distance_ready, (KH - KD) * f + k - KD + 1)
                    nc.scalar.activation(onehot[:, f % 2, k, :], distance[:, k - KD, :], ACT.Relu,
                                         bias=1.0, scale=-1.0).then_inc(onehot_act, 1)

            def keep_found(f):
                act.wait_ge(found_ready, f + 1)
                copy(extra[:, f, :], spare[:, f % 2, :]).then_inc(found_out, 1)

            act.dma_start(hot_ids_sb[:, 0, :], hot_ids[0:1, :].to_broadcast([HP, B])).then_inc(hot_ids_in[0], 16)
            for f in range(NH):
                if f:
                    place_ids(f)
                split_table(f)
                one_hot(f)
                if f:
                    keep_found(f - 1)
            last_found = NH - 1
            act.wait_ge(found_out, last_found)
            act.wait_ge(dense_in, 16)
            place_columns(0, 0, last_found, 0)
            place_columns(0, DENSE, 1, DENSE)
            place_columns(0, V, COPIES, 0)
            act.wait_ge(found_ready, NH)
            copy(vecs[:, :, :, last_found].rearrange("p h s -> p (h s)"),
                 spare[:, last_found % 2, 0:TILE]).then_inc(extra_cols, 1)
            keep_found(last_found)
            act.wait_ge(found_out, NH)
            act.wait_ge(pairs_free, 1)
            act.wait_ge(small_in, 48)
            with act.Fori(0, TILES - 1) as t:
                vectors(t, 4)
                for m in range(2 * PIECES):
                    products(t, m)
                    if m in (1, 3, 5):
                        vectors(t, {1: 5, 3: 6, 5: 7}[m])
                not_gathered(t + 1)
                mlp(t)
            t = TILES - 1
            for m in range(2 * PIECES):
                products(t, m)
                if m in (0, 2, 4):
                    vectors(t, {0: 4, 2: 5, 4: 6}[m])
                if m == 5:
                    act.wait_ge(last_turned, 1)
                    evacuate(copy, 7, 0, LAST_EARLY).then_inc(last_vecs, 1)
                    act.wait_ge(turned_ready, 8 * TILES)
                    evacuate(copy, 7, LAST_EARLY, PS, bank=0).then_inc(vecs_act, 1)
            mlp(t)


def kernel(**inputs):
    import numpy as np
    import concourse.bacc as bacc
    from concourse.bass_utils import run_bass_kernel_spmd

    x = {name: np.asarray(a) for name, a in inputs.items()}

    def chunked(a):
        return np.ascontiguousarray(a.reshape(-1, CHUNKS, P).transpose(2, 0, 1))

    first = np.cumsum([0] + [VOCABS[f] for f in GATHERED[:-1]]).astype(np.int32)
    w1 = x["W_top1"]
    ref_number = [f + 1 for f in HOT] + [0] + [f + 1 for f in GATHERED]
    pair_row = {pair: r for r, pair in enumerate(zip(*np.triu_indices(V, k=1)))}
    w1_pairs = np.zeros((P, SLOTS, H1), w1.dtype)
    for m in range(1, V):
        for n in range(m):
            if m < LOW:
                at = (n, m - 1)
            else:
                slot, quad = divmod(m - LOW, 4)
                row = V + n if n < 2 and quad == 0 and slot < 2 else n
                at = (QUAD * quad + row, slot)
            w1_pairs[at] = w1[pair_row[tuple(sorted((ref_number[n], ref_number[m])))]]
    n_pairs = V * F // 2
    arrays = {
        "table": np.concatenate([x[f"tbl_{f}"] for f in GATHERED]),
        "ids_and_base": np.concatenate([chunked(x["ids"][:, GATHERED]), chunked(np.tile(first, (HALF, 1)))], axis=1),
        "dense_t": np.ascontiguousarray(x["r_dense"].T),
        "hot_table": np.ascontiguousarray(
            np.stack([x[f"tbl_{f}"].reshape(HP, KH, P) for f in HOT], axis=1)),
        "hot_ids": np.ascontiguousarray(x["ids"][:, HOT].T),
        "hot_rows": np.arange(HP * KH, dtype=np.float32).reshape(HP, KH),
        "w1_pairs": w1_pairs,
        "w1_dense": np.ascontiguousarray(w1[n_pairs:]),
        "b1": np.ascontiguousarray(x["b_top1"].reshape(N1, P).T),
        "w2": np.ascontiguousarray(x["W_top2"].reshape(N1, P, H2).transpose(1, 0, 2)),
        "b2": np.ascontiguousarray(x["b_top2"].reshape(N2, P).T),
        "w3": np.ascontiguousarray(x["W_top3"].reshape(N2, P).T),
    }
    nc = bacc.Bacc("TRN2", target_bir_lowering=False, num_devices=1)
    aps = [nc.dram_tensor(name, a.shape, mybir.dt.from_np(a.dtype), kind="ExternalInput").ap()
           for name, a in arrays.items()]
    y = nc.dram_tensor("y", (1, B), mybir.dt.float32, kind="ExternalOutput").ap()
    program(nc, *aps, y)
    r = run_bass_kernel_spmd(nc, [arrays], core_ids=[0])
    return r.results[0]["y"].reshape(B, 1)
```
